# Optimizing a Trainium2 kernel written in Bass

```python
import numpy as np
import jax
import jax.numpy as jnp

def _softmax(x, axis=-1):
    return jax.nn.softmax(x, axis=axis)

def _gelu(x):
    return jax.nn.gelu(x, approximate=True)

def _silu(x):
    return jax.nn.silu(x)

def _sigmoid(x):
    return jax.nn.sigmoid(x)

def _layernorm(x, axis=-1, eps=1e-05):
    m = jnp.mean(x, axis=axis, keepdims=True)
    v = jnp.var(x, axis=axis, keepdims=True)
    return (x - m) / jnp.sqrt(v + eps)

def _scatter_add(tgt, idx, src, axis=0):
    return tgt.at[idx].add(src)

def _segment_sum(src, seg, n):
    return jax.ops.segment_sum(src, seg, n)
kernel_name = 'mk_gnn_ffn_d2_gnn_r8_b8890d'

def setup_inputs(seed: int=0):
    np.random.seed(seed)
    _w = jnp.asarray

    def _rec_inputs():
        import jax
        import jax.numpy as jnp
        _gk = jax.random.key(seed)
        x = -6.415e-05 + 1 * jax.random.normal(jax.random.fold_in(_gk, 1), (1250, 1024), jnp.float32)
        src = jax.random.randint(jax.random.fold_in(_gk, 2), (40000,), 0, 1250, jnp.int32)
        dst = jnp.minimum((1250 * jax.random.uniform(jax.random.fold_in(_gk, 3), (40000,)) ** 2.0).astype(jnp.int32), 9999)
        _o = jnp.argsort(dst, stable=True)
        src = src[_o]
        dst = dst[_o]
        edge_weight = -0.000130211 + 0.031236 * jax.random.normal(jax.random.fold_in(_gk, 13), (40000,), jnp.float32)
        return (x, src, dst, edge_weight)
    x, src, dst, edge_weight = _rec_inputs()

    def _L0_gnn_setup():
        import jax, jax.numpy as jnp
        import numpy as np
        NEG_SLOPE = 0.1
        EPS = 1e-05
        key = jax.random.key(seed)
        k1, k2, k3, k4, k5 = jax.random.split(key, 5)
        N, E, DIN, DOUT = (1250, 20000, 1024, 1024)
        x = jax.random.normal(k1, (N, DIN), dtype=jnp.float32)
        W = jax.random.normal(k2, (DIN, DOUT), dtype=jnp.float32) * 0.02
        a = jax.random.normal(k3, (1, 2 * DOUT), dtype=jnp.float32) * 0.02
        src = jax.random.randint(k4, (E,), 0, N, dtype=jnp.int64)
        dst = jax.random.randint(k5, (E,), 0, N, dtype=jnp.int64)
        return {'x': x, 'W': W, 'a': a, 'src': src, 'dst': dst}
    _L0_gnn_all = _L0_gnn_setup()
    _L0_gnn_in = {k: v for k, v in _L0_gnn_all.items() if k in ('W', 'a')}
    del _L0_gnn_all

    def _L0_ffn_setup():
        import jax, jax.numpy as jnp
        import numpy as np
        TOP_K = 2
        EPS = 1e-09
        key = jax.random.key(seed)
        ks = jax.random.split(key, 6)
        B, T, D, H, E = (4, 256, 1024, 256, 8)
        x = jax.random.normal(ks[0], (B, T, D), dtype=jnp.float32)
        Wg = jax.random.normal(ks[1], (E, D), dtype=jnp.float32) * 0.02
        W1 = jax.random.normal(ks[2], (E, 2 * H, D), dtype=jnp.float32) * 0.02
        b1 = jax.random.normal(ks[3], (E, 2 * H), dtype=jnp.float32) * 0.02
        Wo = jax.random.normal(ks[4], (D, H), dtype=jnp.float32) * 0.02
        bo = jax.random.normal(ks[5], (D,), dtype=jnp.float32) * 0.02
        return {'x': x, 'Wg': Wg, 'W1': W1, 'b1': b1, 'Wo': Wo, 'bo': bo}
    _L0_ffn_all = _L0_ffn_setup()
    _L0_ffn_in = {k: v for k, v in _L0_ffn_all.items() if k in ('Wg', 'W1', 'b1', 'Wo', 'bo')}
    del _L0_ffn_all

    def _L1_gnn_setup():
        import jax, jax.numpy as jnp
        import numpy as np
        INDIM = 1024
        OUTDIM = 1024
        NNZ = 8192
        N = 6250
        key = jax.random.key(seed)
        k1, k2, k3, k4, k5 = jax.random.split(key, 5)
        x = jax.random.normal(k1, (N, INDIM), dtype=jnp.float32)
        stdv = np.sqrt(6.0 / (INDIM + OUTDIM))
        nnz_weight = jax.random.uniform(k2, (NNZ,), dtype=jnp.float32, minval=-stdv, maxval=stdv)
        bias = jax.random.normal(k3, (OUTDIM,), dtype=jnp.float32) * 0.02
        row = jax.random.randint(k4, (NNZ,), 0, OUTDIM, dtype=jnp.int64)
        col = jax.random.randint(k5, (NNZ,), 0, INDIM, dtype=jnp.int64)
        edge_index = jnp.stack([row, col])
        return {'x': x, 'nnz_weight': nnz_weight, 'bias': bias, 'edge_index': edge_index}
    _L1_gnn_all = _L1_gnn_setup()
    _L1_gnn_in = {k: v for k, v in _L1_gnn_all.items() if k in ('bias',)}
    del _L1_gnn_all

    def _L1_ffn_setup():
        import jax, jax.numpy as jnp
        import numpy as np
        DIM = 1024

        def _reference_tuple_inner(x, W_r, W_k, W_v, mu_r, mu_k):
            B, T, C = x.shape
            x_prev = jnp.concatenate([jnp.zeros((B, 1, C), x.dtype), x[:, :-1, :]], axis=1)
            xr = mu_r * x + (1.0 - mu_r) * x_prev
            xk = mu_k * x + (1.0 - mu_k) * x_prev
            r = jax.nn.sigmoid(jnp.einsum('btc,dc->btd', xr, W_r))
            k = jnp.einsum('btc,dc->btd', xk, W_k)
            k_act = jnp.square(jax.nn.relu(k))
            out = r * jnp.einsum('btc,dc->btd', k_act, W_v)
            new_state = x[:, -1, :]
            return (out, new_state)
        key = jax.random.key(seed)
        ks = jax.random.split(key, 6)
        B, T, C = (8, 256, DIM)
        x = jax.random.normal(ks[0], (B, T, C), dtype=jnp.float32)
        s = 1.0 / np.sqrt(C)
        W_r = jax.random.uniform(ks[1], (C, C), jnp.float32, -s, s)
        W_k = jax.random.uniform(ks[2], (C, C), jnp.float32, -s, s)
        W_v = jax.random.uniform(ks[3], (C, C), jnp.float32, -s, s)
        mu_r = jax.random.uniform(ks[4], (C,), jnp.float32)
        mu_k = jax.random.uniform(ks[5], (C,), jnp.float32)
        return {'x': x, 'W_r': W_r, 'W_k': W_k, 'W_v': W_v, 'mu_r': mu_r, 'mu_k': mu_k}
    _L1_ffn_all = _L1_ffn_setup()
    _L1_ffn_in = {k: v for k, v in _L1_ffn_all.items() if k in ('W_r', 'W_k', 'W_v', 'mu_r', 'mu_k')}
    del _L1_ffn_all
    return {'x': x, 'src': src, 'dst': dst, 'edge_weight': edge_weight, 'L0_gnn_W': _L0_gnn_in['W'], 'L0_gnn_a': _L0_gnn_in['a'], 'L0_ffn_Wg': _L0_ffn_in['Wg'], 'L0_ffn_W1': _L0_ffn_in['W1'], 'L0_ffn_b1': _L0_ffn_in['b1'], 'L0_ffn_Wo': _L0_ffn_in['Wo'], 'L0_ffn_bo': _L0_ffn_in['bo'], 'L1_gnn_bias': _L1_gnn_in['bias'], 'L1_ffn_W_r': _L1_ffn_in['W_r'], 'L1_ffn_W_k': _L1_ffn_in['W_k'], 'L1_ffn_W_v': _L1_ffn_in['W_v'], 'L1_ffn_mu_r': _L1_ffn_in['mu_r'], 'L1_ffn_mu_k': _L1_ffn_in['mu_k']}

def reference(x, src, dst, edge_weight, L0_gnn_W, L0_gnn_a, L0_ffn_Wg, L0_ffn_W1, L0_ffn_b1, L0_ffn_Wo, L0_ffn_bo, L1_gnn_bias, L1_ffn_W_r, L1_ffn_W_k, L1_ffn_W_v, L1_ffn_mu_r, L1_ffn_mu_k):
    import jax
    import jax.numpy as jnp

    def _L0_gnn_ref(x, W, a, src, dst):
        import jax, jax.numpy as jnp
        import numpy as np
        NEG_SLOPE = 0.1
        EPS = 1e-05
        N = x.shape[0]
        d = W.shape[1]
        h = x @ W
        a_l, a_r = (a[0, :d], a[0, d:])
        al = h @ a_l
        ar = h @ a_r
        e = jnp.exp(-jax.nn.leaky_relu(al[src] + ar[dst], negative_slope=NEG_SLOPE))
        rowsum = jax.ops.segment_sum(e, src, num_segments=N)
        h_prime = jax.ops.segment_sum(e[:, None] * h[dst], src, num_segments=N)
        h_prime = h_prime / (rowsum[:, None] + EPS)
        return jax.nn.elu(h_prime)

    def _L0_ffn_ref(x, Wg, W1, b1, Wo, bo):
        import jax, jax.numpy as jnp
        import numpy as np
        TOP_K = 2
        EPS = 1e-09
        E = Wg.shape[0]
        gate_logits = jnp.einsum('btd,ed->bte', x, Wg)
        gate_scores = jax.nn.softmax(gate_logits, axis=-1)
        topk_val, topk_idx = jax.lax.top_k(gate_scores, TOP_K)
        topk_val = topk_val / (topk_val.sum(axis=-1, keepdims=True) + EPS)
        comb = (jax.nn.one_hot(topk_idx, E, dtype=x.dtype) * topk_val[..., None]).sum(axis=-2)
        out = jnp.zeros_like(x)
        for e in range(E):
            h = jnp.einsum('btd,hd->bth', x, W1[e]) + b1[e]
            a, b = jnp.split(h, 2, axis=-1)
            g = a * jax.nn.sigmoid(b)
            eo = jnp.einsum('bth,dh->btd', g, Wo) + bo
            out = out + eo * comb[..., e:e + 1]
        return out

    def _L1_gnn_ref(x, nnz_weight, bias, edge_index):
        import jax, jax.numpy as jnp
        import numpy as np
        INDIM = 1024
        OUTDIM = 1024
        NNZ = 8192
        N = 6250
        row, col = (edge_index[0], edge_index[1])
        W = jnp.zeros((OUTDIM, INDIM), dtype=nnz_weight.dtype).at[row, col].add(nnz_weight)
        return x @ W.T + bias

    def _L1_ffn_ref(x, W_r, W_k, W_v, mu_r, mu_k):
        import jax, jax.numpy as jnp
        import numpy as np
        DIM = 1024

        def _reference_tuple_inner(x, W_r, W_k, W_v, mu_r, mu_k):
            B, T, C = x.shape
            x_prev = jnp.concatenate([jnp.zeros((B, 1, C), x.dtype), x[:, :-1, :]], axis=1)
            xr = mu_r * x + (1.0 - mu_r) * x_prev
            xk = mu_k * x + (1.0 - mu_k) * x_prev
            r = jax.nn.sigmoid(jnp.einsum('btc,dc->btd', xr, W_r))
            k = jnp.einsum('btc,dc->btd', xk, W_k)
            k_act = jnp.square(jax.nn.relu(k))
            out = r * jnp.einsum('btc,dc->btd', k_act, W_v)
            new_state = x[:, -1, :]
            return (out, new_state)
        return _reference_tuple_inner(x, W_r, W_k, W_v, mu_r, mu_k)[0]
    edge_index = jnp.stack([src, dst])
    x = x + _L0_gnn_ref(_layernorm(x, axis=-1), L0_gnn_W, L0_gnn_a, src, dst)
    x = x + _L0_ffn_ref(_layernorm(x, axis=-1)[None], L0_ffn_Wg, L0_ffn_W1, L0_ffn_b1, L0_ffn_Wo, L0_ffn_bo)[0]
    x = x + _L1_gnn_ref(_layernorm(x, axis=-1), edge_weight, L1_gnn_bias, edge_index)
    x = x + _L1_ffn_ref(_layernorm(x, axis=-1)[None], L1_ffn_W_r, L1_ffn_W_k, L1_ffn_W_v, L1_ffn_mu_r, L1_ffn_mu_k)[0]
    return x

_drawn_inputs = setup_inputs


def setup_inputs(seed=0):
    import zlib

    import numpy as np

    out = dict(_drawn_inputs(seed))
    spreads = {}
    factors = {'L0_ffn_b1': 22.728,
     'L0_ffn_bo': 2.743,
     'L1_gnn_bias': 2.817,
     'L1_ffn_W_r': 3.202,
     'L1_ffn_mu_r': 6.625}
    for name, (base, spread) in spreads.items():
        noise = np.random.default_rng([zlib.crc32(name.encode()), seed]).standard_normal(out[name].shape)
        drawn = base * np.exp(spread * noise) if base else spread * noise
        out[name] = jnp.asarray(drawn.astype(out[name].dtype))
    for name, factor in factors.items():
        out[name] = (out[name] * factor).astype(out[name].dtype)
    return out
```

```python
from contextlib import ExitStack

import numpy as np
import concourse.bass as bass
from concourse import mybir

ALU = mybir.AluOpType
ACT = mybir.ActivationFunctionType
AX = mybir.AxisListType
F32 = mybir.dt.float32
F16 = mybir.dt.float16
BF16 = mybir.dt.bfloat16
I32 = mybir.dt.int32

P = 128
BANK = 512
LN_EPS = 1e-5
ROWSUM_EPS = 1e-5
TOPK_EPS = 1e-9
NEG_SLOPE = 0.1
FLT_MAX = 3.4028234e38
RING = 2
OH_RING = 4


def rows_bc(ap, shape):
    return ap.to_broadcast(shape)


def gnn_ffn_kernel(nc, x, src_cols, dst_cols, dst_rows, ew_cols, w0, a, wg_t, w1_t, b1, wo_t, bo, bias,
                   wr_t, wk_t, wv_t, mu_r, mu_k, out):
    N, D = x.shape
    T = -(-N // P)
    LAST = N - (T - 1) * P
    NP = T * P
    KD = D // P
    EP, NCH = src_cols.shape
    NST, EST = dst_rows.shape
    CPS = NCH // NST
    WIN = P // 4
    NWIN = NP // WIN
    HALF = NST // 2
    NE, _, H2 = w1_t.shape
    HID = H2 // 2
    KH = HID // P
    HW = D + 2
    EC = HW // 3
    SRC_CUTS = [(c, min(c + BANK, N)) for c in range(0, N, BANK)]
    assert T % 2 == 0 and HW % 3 == 0 and EC <= BANK and CPS * NST == NCH and NE == 8

    with ExitStack() as ctx:
        def sb(name, shape, dt=F32):
            return ctx.enter_context(nc.sbuf_tensor(name, shape, dt))

        def sem(name):
            return ctx.enter_context(nc.semaphore(name))

        ps = ctx.enter_context(nc.psum_tensor("ps", [P, 8, BANK], F32))

        X = sb("X", [P, T, D])
        hreg = sb("hreg", [P, T * HW])
        a0 = sb("a0", [P, KD * D])
        a1 = sb("a1", [P, KD * D])
        a2 = sb("a2", [P, KD * D])
        xn = sb("xn", [P, RING, D])
        xT = sb("xT", [P, RING, KD, P + 1])
        ident = sb("ident", [P, P])
        al_row = sb("al_row", [P, NP])
        stats = sb("stats", [P, 2, 6])
        mv = sb("mv", [P, 2])
        var_eps = sb("var_eps", [P, 1])
        rstd = sb("rstd", [P, 1])
        neg_half = sb("neg_half", [P, 1])
        alar = sb("alar", [P, 2, T])
        small = sb("small", [P, 8])
        ones_row = sb("ones_row", [1, P])
        zeros = sb("zeros", [P, P], BF16)

        h = hreg[:, :].rearrange("p (t w) -> p t w", t=T)
        w_view = lambda reg: reg[:, 0:KD * D].rearrange("p (k d) -> p k d", k=KD)
        g1 = a1[:, :].bitcast(BF16)
        OH = g1[:, 0:OH_RING * CPS * N].rearrange("p (r c n) -> p r c n", r=OH_RING, c=CPS)
        o = OH_RING * CPS * N
        ST = g1[:, o:o + OH_RING * CPS * P].rearrange("p (r c n) -> p r c n", r=OH_RING, c=CPS)
        o += OH_RING * CPS * P
        iota_s = g1[:, o:o + NP].bitcast(F16)
        o += NP
        WP = g1[:, o:o + 4 * NCH].rearrange("p (c q) -> p c q", q=4)
        o += 4 * NCH
        assert o <= 2 * KD * D
        o = 0
        dump = a2[:, o:o + 2 * N].rearrange("p (r n) -> p r n", r=2)
        o += 2 * N
        src_i = a2[:, o:o + NCH].bitcast(I32)
        dst_i = a2[:, o + NCH:o + 2 * NCH].bitcast(I32)
        o += 2 * NCH
        src_f = a2[:, o:o + NCH]
        dst_f = a2[:, o + NCH:o + 2 * NCH]
        ew_f = a2[:, o + 2 * NCH:o + 3 * NCH]
        part = a2[:, o + 3 * NCH:o + 4 * NCH]
        o += 4 * NCH
        dsr_i = a2[:, o:o + 2 * EST].bitcast(I32).rearrange("p (a e) -> p a e", a=2)
        dsr_f = a2[:, o + 2 * EST:o + 4 * EST].rearrange("p (a e) -> p a e", a=2)
        o += 4 * EST
        mxmn = a2[:, o:o + 4].rearrange("p (m a) -> p m a", m=2)
        mxmn_bc = a2[:, o + 4:o + 4 + 4 * NWIN].rearrange("p (m a w) -> p m a w", m=2, a=2)
        o += 4 + 4 * NWIN
        steps = a2[:, o:o + 2 * NST].rearrange("p (m s) -> p m s", m=2)
        win_lo = a2[:, o + 2 * NST:o + 2 * NST + 1]
        rmask = a2[:, o + 2 * NST + 1:o + 5 * NST + 1].rearrange("p (m s) -> p m s", m=3)
        rng_f = a2[:, o + 5 * NST + 1:o + 5 * NST + 9]
        rng_i = a2[:, o + 5 * NST + 9:o + 5 * NST + 13].bitcast(I32)
        lower = a2[:, o + 5 * NST + 13:o + 5 * NST + 13 + NWIN]
        o += 5 * NST + 13 + NWIN
        assert o <= KD * D
        o = 0
        ET = a2[:, o:o + 2 * T * P].rearrange("p (r k n) -> p r k n", r=2, k=T)
        o += 2 * T * P
        CT = a2[:, o:o + 2 * T * P].rearrange("p (r k n) -> p r k n", r=2, k=T)
        o += 2 * T * P
        hv = a2[:, o:o + HW]
        hm = a2[:, o + HW:o + 2 * HW]
        assert o + 2 * HW <= KD * D
        avec = a1[:, 0:2 * D].rearrange("p (m d) -> p m d", m=2)
        ttr_junk = a1[:, 2 * D:3 * D]
        xT2 = hreg[:, 0:T * D].rearrange("p (t k n) -> p t k n", t=T, k=KD)
        W1 = a1[:, :].rearrange("p (r k n) -> p r k n", r=2, k=KD)
        o = 0
        G = a0[:, 0:T * HID].rearrange("p (t n) -> p t n", t=T)
        o += T * HID
        Wo = a0[:, o:o + KH * D].rearrange("p (k d) -> p k d", k=KH)
        o += KH * D
        SG = a0[:, o:o + 2 * HID].rearrange("p (r n) -> p r n", r=2)
        TM = a0[:, o + 2 * HID:o + 4 * HID].rearrange("p (r n) -> p r n", r=2)
        o += 4 * HID
        GT = a0[:, o:o + 2 * HID].rearrange("p (r k n) -> p r k n", r=2, k=KH)
        o += 2 * HID
        assert o <= KD * D
        wg = sb("wg", [P, KD, NE])
        gat = sb("gat", [P, 8, T, NE])
        gs = sb("gs", [P, 10, T])
        rev = sb("rev", [P, NE])
        b1_row = a2[0:1, 0:NE * H2]
        bo_bc = hreg[:, 0:D]
        WTg = w_view(a2)
        wt2 = hreg[:, 0:KD * D].rearrange("p (k d) -> p k d", k=KD)
        bias_bc = hreg[:, KD * D:(KD + 1) * D]
        Wr, Wk, Wv = w_view(a0), w_view(a1), w_view(hreg)
        xr = a2[:, 0:2 * D].rearrange("p (r k n) -> p r k n", r=2, k=KD)
        xk = a2[:, 2 * D:4 * D].rearrange("p (r k n) -> p r k n", r=2, k=KD)
        xd = a2[:, 4 * D:5 * D].rearrange("p (k n) -> p k n", k=KD)
        kact = a2[:, 5 * D:6 * D]
        kT = a2[:, 6 * D:7 * D].rearrange("p (k n) -> p k n", k=KD)
        rg = a2[:, 7 * D:8 * D]
        rv = hreg[:, KD * D:(KD + 1) * D]
        mu = sb("mu", [P, 2, KD])

        graph_rows = nc.dram_tensor("graph_rows", (4, NP, N), F32, kind="Internal").ap()
        ranges = nc.dram_tensor("ranges", (NWIN, 3), I32, kind="Internal").ap()

        ld_edges, ld_rows, ld_x, ld_w0, ld_a = (sem(s) for s in ("ld_edges", "ld_rows", "ld_x", "ld_w0", "ld_a"))
        ld_small, ld_wo, ld_bo, ld_wt, ld_wt2, ld_bias = (sem(s) for s in (
            "ld_small", "ld_wo", "ld_bo", "ld_wt", "ld_wt2", "ld_bias"))
        ld_w1 = [sem("ld_w1_0"), sem("ld_w1_1")]
        ld_ct = [sem("ld_ct_0"), sem("ld_ct_1")]
        ld_wr, ld_wk, ld_wv = sem("ld_wr"), sem("ld_wk"), sem("ld_wv")
        consts = sem("consts")
        pool_seq, dve_seq, act_seq = sem("pool_seq"), sem("dve_seq"), sem("act_seq")
        mxmn_ready, mxmn_bcast = sem("mxmn_ready"), sem("mxmn_bcast")
        cnt_ready, cnt_sum, rng_ready, rng_stored = sem("cnt_ready"), sem("cnt_sum"), sem("rng_ready"), sem("rng_stored")
        oh_ready, oh_used = sem("oh_ready"), sem("oh_used")
        win_done, win_copied = sem("win_done"), sem("win_copied")
        dump_stored = [sem("dump_stored_0"), sem("dump_stored_1")]
        var_ready, rstd_ready = sem("var_ready"), sem("rstd_ready")
        xn_ready, xn_used, xT_ready = sem("xn_ready"), sem("xn_used"), sem("xT_ready")
        h_acc, h_copied = sem("h_acc"), sem("h_copied")
        alar_ready, al_acc, al_ready = sem("alar_ready"), sem("al_acc"), sem("al_ready")
        z_ready, exp_ready, et_ready, e_acc, e_taken = (sem(s) for s in (
            "z_ready", "exp_ready", "et_ready", "e_acc", "e_taken"))
        neg_ready, elu_exp, x1_ready = sem("neg_ready"), sem("elu_exp"), sem("x1_ready")
        gate_acc, gate_in, gate_exp, comb_ready = sem("gate_acc"), sem("gate_in"), sem("gate_exp"), sem("comb_ready")
        up_acc, sig_ready, up_taken, G_ready = (sem(s) for s in ("up_acc", "sig_ready", "up_taken", "G_ready"))
        gt_acc, gt_ready, down_acc, down_taken = sem("gt_acc"), sem("gt_ready"), sem("down_acc"), sem("down_taken")
        wt_ready, n_acc, n_taken = sem("wt_ready"), sem("n_acc"), sem("n_taken")
        mix_ready, r_acc, r_gate, k_acc, k_act = (sem(s) for s in ("mix_ready", "r_acc", "r_gate", "k_acc", "k_act"))
        kt_acc, kt_ready, v_acc, v_taken, stored = (sem(s) for s in ("kt_acc", "kt_ready", "v_acc", "v_taken", "stored"))
        last_x = sem("last_x")

        def free(n):
            return n + 1

        def done(n, depth=RING):
            return n + 1 + depth

        class Seq:

            def __init__(self, eng, s):
                self.eng, self.s, self.base, self.k = eng, s, 0, 0

            def then(self, ins):
                self.inc(ins)
                self.eng.wait_ge(self.s, self.base + self.k)

            def inc(self, ins):
                ins.then_inc(self.s, 1)
                self.k += 1

            def enter(self, i, per):
                self.start, self.base, self.k, self.per = self.base + self.k, self.base + self.k + per * i, 0, per

            def leave(self, trips):
                assert self.k == self.per, self.k
                self.base, self.k = self.start + self.per * trips, 0

        H0, F0, N0, R0 = 0, T, 2 * T, 3 * T
        block = ctx.enter_context(nc.Block())

        @block.sync
        def _(sp):
            sp.dma_start(src_i[0:EP, :], src_cols).then_inc(ld_edges, 16)
            sp.dma_start(dst_i[0:EP, :], dst_cols).then_inc(ld_edges, 16)
            sp.dma_start(ew_f[0:EP, :], ew_cols).then_inc(ld_edges, 16)
            sp.dma_start(dsr_i[0:HALF, :, :], dst_rows.rearrange("(a p) e -> p a e", a=2)).then_inc(ld_rows, 16)
            sp.wait_ge(consts, 1)
            for t in range(T - 1):
                sp.dma_start(X[:, t, :], x[t * P:(t + 1) * P, :]).then_inc(ld_x, 16)
            sp.dma_start(X[0:LAST, T - 1, :], x[(T - 1) * P:N, :]).then_inc(ld_x, 16)
            sp.dma_start(w_view(a0), w0.rearrange("(k p) d -> p k d", p=P)).then_inc(ld_w0, 16)
            sp.dma_start(wg[:, :, :], wg_t.rearrange("(k p) e -> p k e", p=P)).then_inc(ld_small, 16)
            sp.dma_start(mu[:, 0, :], mu_r).then_inc(ld_small, 16)
            sp.dma_start(mu[:, 1, :], mu_k).then_inc(ld_small, 16)
            sp.wait_ge(rng_ready, 1)
            sp.dma_start(ranges, rng_i[0:NWIN, 0:3]).then_inc(rng_stored, 16)
            with sp.Fori(0, NWIN // 2) as i:
                for b in range(2):
                    at = sp.snap(2 * WIN * i + b * WIN)
                    sp.wait_ge(win_copied, done(2 * i + b))
                    sp.dma_start(graph_rows[:, bass.ds(at, WIN), :], dump[:, b, :]).then_inc(dump_stored[b], 16)
            sp.wait_ge(win_done, NWIN)
            for m in range(2):
                sp.dma_start(avec[:, m, :], a[0:1, m * D:(m + 1) * D].to_broadcast([P, D])).then_inc(ld_a, 16)
            for b in range(2):
                sp.wait_ge(dump_stored[b], 16 * (NWIN // 2))

            def load_counts(s, b, width):
                sp.dma_start(CT[:, b, :, 0:width], graph_rows[0].rearrange("(k p) n -> p k n", p=P)[:, :, s]
                             ).then_inc(ld_ct[b], 16)

            load_counts(slice(0, P), 0, P)
            load_counts(slice(P, 2 * P), 1, P)
            with sp.Fori(0, T // 2 - 2) as i:
                for b in range(2):
                    at = sp.snap(2 * P * i + (2 + b) * P)
                    sp.wait_ge(et_ready, 2 * i + b + 1)
                    load_counts(bass.ds(at, P), b, P)
            sp.wait_ge(et_ready, T - 3)
            load_counts(slice((T - 2) * P, (T - 1) * P), 0, P)
            sp.wait_ge(et_ready, T - 2)
            load_counts(slice((T - 1) * P, N), 1, LAST)
            sp.wait_ge(alar_ready, T)
            for b in range(2):
                sp.dma_start(W1[:, b, :, :], w1_t[b].rearrange("(k p) n -> p k n", p=P)).then_inc(ld_w1[b], 16)
            sp.dma_start(Wo, wo_t.rearrange("(k p) d -> p k d", p=P)).then_inc(ld_wo, 16)
            sp.wait_ge(x1_ready, T)
            sp.dma_start(b1_row, b1.rearrange("(a e) n -> a (e n)", a=1)).then_inc(ld_small, 16)
            with sp.Fori(0, NE // 2 - 1) as i:
                for b in range(2):
                    e = sp.snap(2 * i + 2 + b)
                    sp.wait_ge(up_acc, T * (2 * i + b + 1))
                    sp.dma_start(W1[:, b, :, :], w1_t[bass.ds(e, 1)].rearrange("a (k p) n -> p (a k) n", p=P)
                                 ).then_inc(ld_w1[b], 16)
            sp.wait_ge(up_acc, T * NE)
            sp.dma_start(bo_bc, bo.to_broadcast([P, D])).then_inc(ld_bo, 16)
            for g in (1, 2, 3):
                rows = graph_rows[g].rearrange("(k p) n -> p k n", p=P)[:, 0:KD, 0:D]
                if g == 1:
                    sp.dma_start(WTg, rows).then_inc(ld_wt, 16)
                    sp.dma_start(w_view(a1), wk_t.rearrange("(k p) d -> p k d", p=P)).then_inc(ld_wk, 16)
                else:
                    if g == 2:
                        sp.wait_ge(down_taken, T)
                    else:
                        sp.wait_ge(wt_ready, 1)
                    sp.dma_start(wt2, rows).then_inc(ld_wt2, 16)
            sp.dma_start(bias_bc, bias.to_broadcast([P, D])).then_inc(ld_bias, 16)
            sp.dma_start(w_view(a0), wr_t.rearrange("(k p) d -> p k d", p=P)).then_inc(ld_wr, 16)
            sp.wait_ge(wt_ready, 2)
            sp.dma_start(Wv, wv_t.rearrange("(k p) d -> p k d", p=P)).then_inc(ld_wv, 16)
            with sp.Fori(0, T - 1) as t:
                at = sp.snap(t * P)
                sp.wait_ge(last_x, t + 1)
                sp.dma_start(out[bass.ds(at, P), :], X[:, bass.ds(t, 1), :].rearrange("p a d -> p (a d)")
                             ).then_inc(stored, 16)
            sp.wait_ge(last_x, T)
            sp.dma_start(out[(T - 1) * P:N, :], X[0:LAST, T - 1, :]).then_inc(stored, 16)
            sp.wait_ge(stored, 16 * T)

        @block.gpsimd
        def _(pool):
            seq = Seq(pool, pool_seq)
            pl = nc.gpsimd
            first = (LAST // 32) * 32
            pl.memset(X[first:P, T - 1, :], 0.0).then_inc(consts, 1)
            pool.wait_ge(consts, 1)
            seq.then(pl.memset(ident[:, :], 0.0))
            pl.affine_select(out=ident[:, :], in_=ident[:, :], compare_op=ALU.not_equal, fill=1.0, base=0,
                             pattern=[[-1, P]], channel_multiplier=1).then_inc(pool_seq, 1)
            pl.iota(iota_s[:, :], [[1, NP]], base=0, channel_multiplier=0,
                    allow_small_or_imprecise_dtypes=True).then_inc(pool_seq, 1)
            pl.iota(steps[:, 0, :], [[-1, NST]], base=NST, channel_multiplier=0,
                    allow_small_or_imprecise_dtypes=True).then_inc(pool_seq, 1)
            pl.iota(steps[:, 1, :], [[1, NST]], base=1, channel_multiplier=0,
                    allow_small_or_imprecise_dtypes=True).then_inc(pool_seq, 1)
            pl.iota(win_lo, [[0, 1]], base=0, channel_multiplier=WIN,
                    allow_small_or_imprecise_dtypes=True).then_inc(pool_seq, 1)
            pl.iota(rev[:, :], [[-1, NE]], base=NE, channel_multiplier=0,
                    allow_small_or_imprecise_dtypes=True).then_inc(pool_seq, 1)
            seq.then(pl.memset(lower[:, :], 1.0))
            seq.k += 6
            pool.wait_ge(pool_seq, 8)
            seq.then(pl.affine_select(out=lower[:, :], in_=lower[:, :], compare_op=ALU.is_gt, fill=0.0, base=0,
                                      pattern=[[1, NWIN]], channel_multiplier=-1))
            pl.memset(ones_row[:, :], 1.0).then_inc(pool_seq, 1)
            pl.memset(neg_half[:, :], -0.5).then_inc(pool_seq, 1)
            pl.memset(zeros[:, :], 0.0).then_inc(pool_seq, 1)
            pl.memset(xT[:, 0, :, 0:1], 0.0).then_inc(pool_seq, 1)
            pool.wait_ge(pool_seq, 13)
            pool.sem_inc(consts, 1)
            with pool.Fori(0, 4 * T) as n:
                pool.wait_ge(var_ready, n + 1)
                pl.tensor_tensor(rstd[:, :], var_eps[:, :], neg_half[:, :], ALU.pow).then_inc(rstd_ready, 1)

        @block.scalar
        def _(act):
            sc = nc.scalar
            act.sem_inc(win_copied, 2)
            act.sem_inc(xT_ready, 1)
            act.sem_inc(h_copied, RING)
            act.sem_inc(r_gate, 1)
            act.sem_inc(k_act, 1)

            def copy_xT(n, b, dst=None, taken=None, value=0):
                act.wait_ge(xn_used, done(n))
                if taken is not None:
                    act.wait_ge(taken, value)
                sc.copy(xT[:, b, :, 1:P + 1] if dst is None else dst,
                        ps[:, 6:8, :].rearrange("p a (k n) -> p (a k) n", n=P)).then_inc(xT_ready, 1)

            with act.Fori(0, NWIN // 2) as i:
                for b in range(2):
                    act.wait_ge(win_done, 2 * i + b + 1)
                    act.wait_ge(dump_stored[b], 16 * i)
                    src = ps[:, 3 * b:3 * b + 3, :].rearrange("p a n -> p (a n)")[:, 0:N]
                    sc.copy(dump[:, b, :], src).then_inc(win_copied, 1)

            def copy_h(t, b):
                act.wait_ge(h_acc, done(t))
                sc.copy(h[:, bass.ds(t, 1), 0:D].rearrange("p a d -> p (a d)"),
                        ps[:, 2 * b:2 * b + 2, :].rearrange("p a n -> p (a n)")).then_inc(h_copied, 1)

            copy_xT(0, 0)
            with act.Fori(0, T // 2 - 1) as i:
                copy_xT(2 * i + 1, 1, taken=h_acc, value=free(2 * i + 1))
                copy_h(2 * i, 0)
                copy_xT(2 * i + 2, 0, taken=h_acc, value=free(2 * i + 2))
                copy_h(2 * i + 1, 1)
            copy_xT(T - 1, 1, taken=h_acc, value=free(T - 1))
            copy_h(T - 2, 0)
            copy_h(T - 1, 1)
            act.wait_ge(al_acc, 1)
            sc.copy(al_row[:, :], ps[:, 0:3, :].rearrange("p a n -> p (a n)")[:, 0:NP]).then_inc(al_ready, 1)

            def exp_scores(s, b):
                act.wait_ge(z_ready, s + 1)
                sc.activation(ET[:, b, :, :], ET[:, b, :, :], ACT.Exp, scale=-1.0).then_inc(exp_ready, 1)

            def exp_elu(s):
                act.wait_ge(neg_ready, s + 1)
                sc.activation(hm, hm, ACT.Exp).then_inc(elu_exp, 1)

            exp_scores(0, 0)
            with act.Fori(0, T // 2 - 1) as i:
                for j in range(2):
                    exp_scores(2 * i + j + 1, (j + 1) % 2)
                    exp_elu(2 * i + j)
            exp_scores(T - 1, 1)
            exp_elu(T - 2)
            exp_elu(T - 1)

            for t in range(T):
                copy_xT(F0 + t, t % 2, xT2[:, t, :, :])
            act.wait_ge(gate_in, 1)
            sc.activation(gat[:, 1, :, :], gat[:, 1, :, :], ACT.Exp).then_inc(gate_exp, 1)
            with act.Fori(0, NE) as e:
                for t in range(T):
                    act.wait_ge(up_acc, T * e + t + 1)
                    act.wait_ge(up_taken, T * e + t + 4)
                    sc.activation(SG[:, t % 2, :], ps[:, t % 5, HID:H2], ACT.Sigmoid).then_inc(sig_ready, 1)
            for t in range(T):
                act.wait_ge(gt_acc, t + 1)
                if t >= 2:
                    act.wait_ge(down_acc, t - 1)
                sc.copy(GT[:, t % 2, :, :].rearrange("p k n -> p (k n)"), ps[:, 6 + t % 2, 0:HID]).then_inc(gt_ready, 1)

            copy_xT(N0, 0)
            with act.Fori(0, T // 2 - 1) as i:
                copy_xT(N0 + 2 * i + 1, 1, taken=n_acc, value=free(2 * i + 1))
                copy_xT(N0 + 2 * i + 2, 0, taken=n_acc, value=free(2 * i + 2))
            copy_xT(N0 + T - 1, 1, taken=n_acc, value=free(T - 1))

            def gates(t):
                act.wait_ge(r_acc, t + 1)
                act.wait_ge(v_taken, t + 1)
                sc.activation(rg, ps[:, 0:2, :].rearrange("p a n -> p (a n)"), ACT.Sigmoid).then_inc(r_gate, 1)

            def squares(t):
                act.wait_ge(k_acc, done(t))
                act.wait_ge(kt_acc, t + 1)
                sc.activation(kact, ps[:, 2:4, :].rearrange("p a n -> p (a n)"), ACT.Relu).then_inc(act_seq, 1)
                act.wait_ge(act_seq, t + 1)
                sc.activation(kact, kact, ACT.Square).then_inc(k_act, 1)

            def copy_kT(t):
                act.wait_ge(kt_acc, t + 2)
                act.wait_ge(v_acc, t + 1)
                sc.copy(kT, ps[:, 4:6, :].rearrange("p a (k n) -> p (a k) n", n=P)).then_inc(kt_ready, 1)

            copy_xT(R0, 0)
            copy_xT(R0 + 1, 1, taken=n_acc, value=done(T - 1))
            gates(0)
            squares(0)
            with act.Fori(0, T // 2 - 1) as i:
                for j in range(2):
                    copy_xT(R0 + 2 * i + j + 2, j, taken=mix_ready, value=2 * i + j + 2)
                    copy_kT(2 * i + j)
                    gates(2 * i + j + 1)
                    squares(2 * i + j + 1)
            copy_kT(T - 2)
            gates(T - 1)
            squares(T - 1)
            copy_kT(T - 1)

        @block.vector
        def _(dve):
            v = nc.vector
            seq = Seq(dve, dve_seq)
            dve.wait_ge(ld_rows, 16)
            seq.then(v.tensor_copy(dsr_f[0:HALF], dsr_i[0:HALF]))
            v.tensor_reduce(mxmn[0:HALF, 0, :], dsr_f[0:HALF], AX.X, ALU.max).then_inc(mxmn_ready, 1)
            v.tensor_reduce(mxmn[0:HALF, 1, :], dsr_f[0:HALF], AX.X, ALU.min).then_inc(mxmn_ready, 1)
            dve.wait_ge(mxmn_ready, 2)
            dve.wait_ge(consts, 2)
            for m in range(2):
                for c in range(2):
                    v.tensor_copy(mxmn_bc[0:HALF, m, c, :], mxmn[0:HALF, m, c:c + 1].to_broadcast([HALF, NWIN])
                                  ).then_inc(mxmn_ready, 1)
            dve.wait_ge(ld_edges, 48)
            seq.then(v.tensor_copy(src_f[0:EP], src_i[0:EP]))
            seq.then(v.tensor_copy(dst_f[0:EP], dst_i[0:EP]))
            seq.then(v.memset(WP[0:EP, :, 0], 1.0))
            seq.then(v.tensor_copy(WP[0:EP, :, 1], ew_f[0:EP]))
            seq.then(v.tensor_tensor(part[0:EP], ew_f[0:EP], WP[0:EP, :, 1], ALU.subtract))
            seq.then(v.tensor_copy(WP[0:EP, :, 2], part[0:EP]))
            seq.then(v.tensor_tensor(part[0:EP], part[0:EP], WP[0:EP, :, 2], ALU.subtract))
            seq.then(v.tensor_copy(WP[0:EP, :, 3], part[0:EP]))
            dve.wait_ge(mxmn_bcast, 1)
            W = slice(0, NWIN)
            mx, mn = ps[W, 6, 0:NST], ps[W, 6, NST:2 * NST]
            seq.then(v.tensor_scalar(rmask[W, 0], mn, float(1 - WIN), win_lo[W], ALU.add, ALU.is_le))
            seq.then(v.scalar_tensor_tensor(out=rmask[W, 0], in0=mx, scalar=win_lo[W], in1=rmask[W, 0],
                                            op0=ALU.is_ge, op1=ALU.mult))
            seq.then(v.tensor_tensor(rmask[W, 1:3], steps[W], rmask[W, 0:1].to_broadcast([NWIN, 2, NST]), ALU.mult))
            seq.then(v.tensor_reduce(rng_f[W, 0:2], rmask[W, 1:3], AX.X, ALU.max))
            seq.then(v.tensor_scalar(rng_f[W, 2:3], rng_f[W, 0:1], -1.0, float(NST), ALU.mult, ALU.add))
            seq.then(v.tensor_scalar(rng_f[W, 2:3], rng_f[W, 2:3], float(NST - 1), None, ALU.min))
            seq.then(v.tensor_tensor(rng_f[W, 3:4], rng_f[W, 1:2], rng_f[W, 2:3], ALU.subtract))
            v.tensor_scalar(rng_f[W, 3:4], rng_f[W, 3:4], 1.0, None, ALU.max).then_inc(cnt_ready, 1)
            dve.wait_ge(cnt_ready, 1)
            dve.wait_ge(cnt_sum, 1)
            seq.then(v.tensor_copy(rng_f[W, 4:5], ps[W, 7, 0:1]))
            seq.then(v.tensor_tensor(rng_f[W, 5:6], rng_f[W, 4:5], rng_f[W, 3:4], ALU.add))
            seq.then(v.tensor_tensor(rng_f[W, 6:7], rng_f[W, 2:3], rng_f[W, 4:5], ALU.subtract))
            seq.then(v.tensor_scalar(rng_f[W, 6:7], rng_f[W, 6:7], float(NWIN * NST), None, ALU.add))
            v.tensor_copy(rng_i[W, 0:3], rng_f[W, 4:7]).then_inc(rng_ready, 1)

            dve.wait_ge(rng_stored, 16)
            with dve.Fori(0, NWIN) as w:
                n0 = dve.value_load(ranges[bass.ds(w, 1), 0:1], min_val=0, max_val=NWIN * NST)
                n1 = dve.value_load(ranges[bass.ds(w, 1), 1:2], min_val=1, max_val=NWIN * NST)
                sh = dve.value_load(ranges[bass.ds(w, 1), 2:3], min_val=0, max_val=2 * NWIN * NST)
                with dve.Fori(n0, n1) as n:
                    st = nc.s_assert_within(dve.snap(n + sh - NWIN * NST), 0, NST - 1,
                                            skip_runtime_bounds_check_because="n runs over the window's steps")
                    r = dve.snap(n % OH_RING)
                    dve.wait_ge(oh_used, free(n))
                    for c in range(CPS):
                        v.tensor_scalar(OH[0:EP, bass.ds(r, 1), c, :].rearrange("p a n -> p (a n)"), iota_s[0:EP, 0:N],
                                        src_f[0:EP, bass.ds(st * CPS + c, 1)], None, ALU.is_equal)
                        ins = v.scalar_tensor_tensor(
                            out=ST[0:EP, bass.ds(r, 1), c, :].rearrange("p a (q n) -> p (a q) n", q=4),
                            in0=iota_s[0:EP, bass.ds(w * WIN, WIN)].rearrange("p (a n) -> p a n", a=1).to_broadcast([EP, 4, WIN]),
                            scalar=dst_f[0:EP, bass.ds(st * CPS + c, 1)],
                            in1=WP[0:EP, bass.ds(st * CPS + c, 1), :].rearrange("p a (q b) -> p (a q) b", b=1).to_broadcast([EP, 4, WIN]),
                            op0=ALU.is_equal, op1=ALU.mult)
                    ins.then_inc(oh_ready, 1)

            def norm(n, t, b):
                xt = X[:, bass.ds(t, 1), :].rearrange("p a d -> p (a d)")
                seq.inc(v.bn_stats(stats[:, 0, :], xt[:, 0:D // 2]))
                seq.then(v.bn_stats(stats[:, 1, :], xt[:, D // 2:D]))
                seq.inc(v.memset(var_eps[:, :], LN_EPS))
                seq.then(v.bn_aggr(mv[:, :], stats[:, :, :].rearrange("p a s -> p (a s)")))
                v.tensor_tensor(var_eps[:, :], var_eps[:, :], mv[:, 1:2], ALU.add).then_inc(var_ready, 1)
                dve.wait_ge(rstd_ready, n + 1)
                dve.wait_ge(xn_used, free(n))
                v.tensor_scalar(xn[:, b, :], xt, mv[:, 0:1], rstd[:, 0:1], ALU.subtract, ALU.mult
                                ).then_inc(xn_ready, 1)

            def dots(t):
                dve.wait_ge(h_copied, done(t))
                for m in range(2):
                    seq.then(v.tensor_tensor(ttr_junk, h[:, bass.ds(t, 1), 0:D].rearrange("p a d -> p (a d)"),
                                             avec[:, m, :], ALU.mult))
                    ins = v.tensor_reduce(alar[:, m, bass.ds(t, 1)], ttr_junk, AX.X, ALU.add)
                    if m == 0:
                        seq.then(ins)
                    else:
                        ins.then_inc(alar_ready, 1)
                        dve.wait_ge(alar_ready, t + 1)

            dve.wait_ge(ld_x, 16 * T)
            norm(0, 0, 0)
            dve.wait_ge(ld_a, 32)
            v.memset(h[:, :, D:D + 1], 1.0)
            seq.then(v.memset(h[:, :, D + 1:D + 2], 0.0))
            with dve.Fori(0, T // 2 - 1) as i:
                seq.enter(i, 14)
                norm(2 * i + 1, 2 * i + 1, 1)
                dots(2 * i)
                norm(2 * i + 2, 2 * i + 2, 0)
                dots(2 * i + 1)
                seq.leave(T // 2 - 1)
            norm(T - 1, T - 1, 1)
            dots(T - 2)
            dots(T - 1)

            def scores(s, b):
                dve.wait_ge(e_acc, free(s))
                seq.then(v.tensor_tensor(ET[:, b, :, :],
                                         al_row[:, bass.ds(s * P, P)].rearrange("p (a n) -> p a n", a=1).to_broadcast([P, T, P]),
                                         alar[:, 1, :].rearrange("p (t a) -> p t a", a=1).to_broadcast([P, T, P]), ALU.add))
                v.scalar_tensor_tensor(out=ET[:, b, :, :], in0=ET[:, b, :, :], scalar=NEG_SLOPE, in1=ET[:, b, :, :],
                                       op0=ALU.mult, op1=ALU.max).then_inc(z_ready, 1)

            def weigh(s, b, wait_ct):
                dve.wait_ge(exp_ready, s + 1)
                dve.wait_ge(ld_ct[b], wait_ct)
                v.scalar_tensor_tensor(out=ET[:, b, :, :], in0=ET[:, b, :, :], scalar=FLT_MAX, in1=CT[:, b, :, :],
                                       op0=ALU.min, op1=ALU.mult).then_inc(et_ready, 1)

            def attend(s, b):
                dve.wait_ge(e_acc, done(s))
                acc = ps[:, 3 * b:3 * b + 3, 0:EC]
                seq.then(v.tensor_scalar(small[:, 0:1], ps[:, 3 * b + 2, D - 2 * EC:D - 2 * EC + 1], ROWSUM_EPS, None, ALU.add))
                seq.then(v.reciprocal(small[:, 1:2], small[:, 0:1]))
                v.tensor_scalar(hv.rearrange("p (a n) -> p a n", a=3), acc, small[:, 1:2], None, ALU.mult
                                ).then_inc(e_taken, 1)
                dve.wait_ge(e_taken, done(s))
                v.tensor_scalar(hm, hv, 0.0, None, ALU.min).then_inc(neg_ready, 1)
                dve.wait_ge(elu_exp, s + 1)
                seq.then(v.scalar_tensor_tensor(out=hv, in0=hm, scalar=-1.0, in1=hv, op0=ALU.add, op1=ALU.max))
                xt = X[:, bass.ds(s, 1), :].rearrange("p a d -> p (a d)")
                v.tensor_tensor(xt, xt, hv[:, 0:D], ALU.add).then_inc(x1_ready, 1)

            dve.sem_inc(e_taken, RING)
            dve.wait_ge(al_ready, 1)
            scores(0, 0)
            weigh(0, 0, 16)
            with dve.Fori(0, T // 2 - 1) as i:
                seq.enter(i, 8)
                for j in range(2):
                    scores(2 * i + j + 1, (j + 1) % 2)
                    weigh(2 * i + j + 1, (j + 1) % 2, 16 * (i + 1 + j))
                    attend(2 * i + j, j)
                seq.leave(T // 2 - 1)
            scores(T - 1, 1)
            weigh(T - 1, 1, 16 * (T // 2))
            attend(T - 2, 0)
            attend(T - 1, 1)

            dve.wait_ge(x1_ready, T)
            for t in range(T):
                norm(F0 + t, t, t % 2)
            dve.wait_ge(gate_acc, T)
            L, E1, E2, E3 = (gat[:, k, :, :] for k in (0, 1, 2, 3))
            bc = lambda k: gs[:, k, :].rearrange("p (t a) -> p t a", a=1).to_broadcast([P, T, NE])
            revb = rev[:, :].rearrange("p (a e) -> p a e", a=1).to_broadcast([P, T, NE])
            seq.then(v.tensor_copy(L, ps[:, 5, 0:T * NE].rearrange("p (t e) -> p t e", t=T)))
            seq.then(v.tensor_reduce(gs[:, 0, :], L, AX.X, ALU.max))
            v.tensor_tensor(E1, L, bc(0), ALU.subtract).then_inc(gate_in, 1)
            dve.wait_ge(gate_exp, 1)
            seq.then(v.tensor_reduce(gs[:, 1, :], E1, AX.X, ALU.add))
            seq.then(v.reciprocal(gs[:, 2, :], gs[:, 1, :]))
            seq.then(v.tensor_tensor(E1, E1, bc(2), ALU.mult))

            def top(scores_, k, onehot):
                seq.then(v.tensor_reduce(gs[:, k, :], scores_, AX.X, ALU.max))
                seq.then(v.tensor_tensor(onehot, scores_, bc(k), ALU.is_equal))
                seq.then(v.tensor_tensor(onehot, onehot, revb, ALU.mult))
                seq.then(v.tensor_reduce(gs[:, 5, :], onehot, AX.X, ALU.max))
                seq.then(v.tensor_tensor(onehot, onehot, bc(5), ALU.is_equal))

            top(E1, 3, E2)
            seq.then(v.scalar_tensor_tensor(out=L, in0=E2, scalar=-2.0, in1=E1, op0=ALU.mult, op1=ALU.add))
            top(L, 4, E3)
            seq.then(v.tensor_tensor(gs[:, 6, :], gs[:, 3, :], gs[:, 4, :], ALU.add))
            seq.then(v.tensor_scalar(gs[:, 7, :], gs[:, 6, :], TOPK_EPS, None, ALU.add))
            seq.then(v.reciprocal(gs[:, 8, :], gs[:, 7, :]))
            seq.then(v.tensor_tensor(gs[:, 9, :], gs[:, 6, :], gs[:, 8, :], ALU.mult))
            seq.then(v.tensor_tensor(E2, E2, bc(3), ALU.mult))
            seq.then(v.tensor_tensor(E3, E3, bc(4), ALU.mult))
            seq.then(v.tensor_tensor(E2, E2, E3, ALU.add))
            seq.then(v.tensor_tensor(E2, E2, bc(8), ALU.mult))
            seq.then(v.memset(G, 0.0))
            dve.sem_inc(up_taken, 5)
            with dve.Fori(0, NE) as e:
                seq.enter(e, T)
                for t in range(T):
                    dve.wait_ge(sig_ready, T * e + t + 1)
                    v.scalar_tensor_tensor(out=TM[:, t % 2, :], in0=ps[:, t % 5, 0:HID],
                                           scalar=gat[:, 2, t, bass.ds(e, 1)], in1=SG[:, t % 2, :],
                                           op0=ALU.mult, op1=ALU.mult).then_inc(up_taken, 1)
                    dve.wait_ge(up_taken, T * e + t + 6)
                    seq.then(v.tensor_tensor(G[:, t, :], G[:, t, :], TM[:, t % 2, :], ALU.add))
                seq.leave(NE)
            dve.sem_inc(G_ready, 1)
            dve.wait_ge(ld_bo, 16)
            for t in range(T):
                dve.wait_ge(down_acc, t + 1)
                acc = ps[:, 2 * (t % 2):2 * (t % 2) + 2, :].rearrange("p a n -> p (a n)")
                seq.then(v.tensor_tensor(X[:, t, :], X[:, t, :], acc, ALU.add))
                v.scalar_tensor_tensor(out=X[:, t, :], in0=bo_bc, scalar=gs[:, 9, t:t + 1], in1=X[:, t, :],
                                       op0=ALU.mult, op1=ALU.add).then_inc(down_taken, 1)
            dve.wait_ge(down_taken, T)

            norm(N0, 0, 0)
            dve.wait_ge(ld_wt, 16)
            dve.wait_ge(ld_wt2, 16)
            v.tensor_tensor(WTg, WTg, wt2, ALU.add).then_inc(wt_ready, 1)
            dve.wait_ge(wt_ready, 1)
            dve.wait_ge(ld_wt2, 32)
            v.tensor_tensor(WTg, WTg, wt2, ALU.add).then_inc(wt_ready, 1)
            dve.wait_ge(ld_bias, 16)

            def add_graph(t, b):
                dve.wait_ge(n_acc, done(t))
                xt = X[:, bass.ds(t, 1), :].rearrange("p a d -> p (a d)")
                v.tensor_tensor(xt, xt, ps[:, 2 * b:2 * b + 2, :].rearrange("p a n -> p (a n)"), ALU.add
                                ).then_inc(n_taken, 1)
                dve.wait_ge(n_taken, done(t))
                seq.then(v.tensor_tensor(xt, xt, bias_bc, ALU.add))

            dve.sem_inc(n_taken, RING)
            with dve.Fori(0, T // 2 - 1) as i:
                seq.enter(i, 10)
                norm(N0 + 2 * i + 1, 2 * i + 1, 1)
                add_graph(2 * i, 0)
                norm(N0 + 2 * i + 2, 2 * i + 2, 0)
                add_graph(2 * i + 1, 1)
                seq.leave(T // 2 - 1)
            norm(N0 + T - 1, T - 1, 1)
            add_graph(T - 2, 0)
            add_graph(T - 1, 1)

            def mix(t, b, first=False):
                dve.wait_ge(xT_ready, R0 + t + 2)
                dve.wait_ge(k_acc, free(t))
                if not first:
                    seq.then(v.tensor_copy(xT[:, b, :, 0:1], xT[:, 1 - b, :, P:P + 1]))
                now, before = xT[:, b, :, 1:P + 1], xT[:, b, :, 0:P]
                seq.then(v.tensor_tensor(xd, now, before, ALU.subtract))
                for m, dst in ((0, xr), (1, xk)):
                    seq.then(v.tensor_tensor(dst[:, b], xd, mu[:, m, :].rearrange("p (k a) -> p k a", a=1).to_broadcast([P, KD, P]),
                                             ALU.mult))
                    ins = v.tensor_tensor(dst[:, b], dst[:, b], before, ALU.add)
                    if m == 0:
                        seq.then(ins)
                    else:
                        ins.then_inc(mix_ready, 1)
                        dve.wait_ge(mix_ready, t + 1)

            def finish(t):
                dve.wait_ge(v_acc, t + 2)
                dve.wait_ge(r_gate, t + 2)
                v.tensor_tensor(rv, rg, ps[:, 4:6, :].rearrange("p a n -> p (a n)"), ALU.mult).then_inc(v_taken, 1)
                dve.wait_ge(v_taken, t + 2)
                xt = X[:, bass.ds(t, 1), :].rearrange("p a d -> p (a d)")
                v.tensor_tensor(xt, xt, rv, ALU.add).then_inc(last_x, 1)
                dve.wait_ge(last_x, t + 1)

            dve.sem_inc(v_taken, 1)
            norm(R0, 0, 0)
            mix(0, 0, first=True)
            norm(R0 + 1, 1, 1)
            mix(1, 1)
            with dve.Fori(0, T // 2 - 1) as i:
                seq.enter(i, 18)
                for j in range(2):
                    norm(R0 + 2 * i + j + 2, 2 * i + j + 2, j)
                    mix(2 * i + j + 2, j)
                    finish(2 * i + j)
                seq.leave(T // 2 - 1)
            finish(T - 2)
            finish(T - 1)

        @block.tensor
        def _(pe):
            mm = nc.tensor.matmul
            pe.sem_inc(oh_used, OH_RING)
            pe.sem_inc(xn_used, RING)
            pe.sem_inc(h_acc, RING)
            pe.sem_inc(e_acc, RING)
            pe.sem_inc(n_acc, RING)
            pe.sem_inc(k_acc, RING)
            pe.sem_inc(kt_acc, 1)
            pe.sem_inc(v_acc, 1)
            pe.wait_ge(mxmn_ready, 6)
            for m in range(2):
                for c in range(2):
                    last = mm(ps[0:NWIN, 6, m * NST + c * HALF:m * NST + (c + 1) * HALF], mxmn_bc[0:HALF, m, c, :],
                              ident[0:HALF, 0:HALF], start=True, stop=True)
            last.then_inc(mxmn_bcast, 1)
            pe.wait_ge(cnt_ready, 1)
            mm(ps[0:NWIN, 7, 0:1], lower[0:NWIN, :], rng_f[0:NWIN, 3:4], start=True, stop=True).then_inc(cnt_sum, 1)

            pe.wait_ge(rng_stored, 16)
            with pe.Fori(0, NWIN // 2) as i:
                for b in range(2):
                    n0 = pe.value_load(ranges[bass.ds(2 * i + b, 1), 0:1], min_val=0, max_val=NWIN * NST)
                    n1 = pe.value_load(ranges[bass.ds(2 * i + b, 1), 1:2], min_val=1, max_val=NWIN * NST)
                    pe.wait_ge(win_copied, 2 * i + b + 1)
                    for j in range(3):
                        mm(ps[:, 3 * b + j, 0:2], zeros[:, :], zeros[:, 0:2], start=True, stop=True)
                    with pe.Fori(n0, n1) as n:
                        r = pe.snap(n % OH_RING)
                        pe.wait_ge(oh_ready, n + 1)
                        for c in range(CPS):
                            for j, (lo, hi) in enumerate(SRC_CUTS):
                                last = mm(ps[:, 3 * b + j, 0:hi - lo],
                                          ST[0:EP, bass.ds(r, 1), c, :].rearrange("p a n -> p (a n)"),
                                          OH[0:EP, bass.ds(r, 1), c, lo:hi].rearrange("p a n -> p (a n)"),
                                          start=False, stop=True, skip_group_check=True)
                        last.then_inc(oh_used, 1)
                    mm(ps[:, 7, 0:2], zeros[:, :], zeros[:, 0:2], start=True, stop=True).then_inc(win_done, 1)

            def turn(n, b):
                pe.wait_ge(xn_ready, n + 1)
                pe.wait_ge(xT_ready, n + 1)
                for k in range(KD):
                    last = nc.tensor.transpose(ps[:, 6 + k // 4, (k % 4) * P:(k % 4 + 1) * P],
                                               xn[:, b, k * P:(k + 1) * P], ident[:, :])
                last.then_inc(xn_used, 1)

            def product(bank, lhs, rhs, k_tiles):
                for half in range(2):
                    for k in range(k_tiles):
                        last = mm(ps[:, bank + half, :], lhs(k), rhs[:, k, half * BANK:(half + 1) * BANK],
                                  start=(k == 0), stop=(k == k_tiles - 1))
                return last

            def x_rows(b):
                return lambda k: xT[:, b, k, 1:P + 1]

            def project(t, n, b, w, taken, acc):
                pe.wait_ge(xT_ready, n + 2)
                pe.wait_ge(taken, free(t))
                product(2 * b, x_rows(b), w, KD).then_inc(acc, 1)

            def token_loop(base, w, taken, acc):
                turn(base, 0)
                with pe.Fori(0, T // 2 - 1) as i:
                    for j in range(2):
                        turn(base + 2 * i + j + 1, (j + 1) % 2)
                        project(2 * i + j, base + 2 * i + j, j, w, taken, acc)
                turn(base + T - 1, 1)
                project(T - 2, base + T - 2, 0, w, taken, acc)
                project(T - 1, base + T - 1, 1, w, taken, acc)

            pe.wait_ge(ld_w0, 16)
            pe.wait_ge(win_copied, NWIN + 2)
            token_loop(H0, w_view(a0), h_copied, h_acc)
            pe.wait_ge(alar_ready, T)
            pe.wait_ge(h_copied, done(T - 1))
            for t in range(T):
                last = mm(ps[:, t // 4, (t % 4) * P:(t % 4 + 1) * P], alar[:, 0, t:t + 1].to_broadcast([P, P]),
                          ident[:, :], start=True, stop=True)
            last.then_inc(al_acc, 1)

            pe.wait_ge(al_ready, 1)
            with pe.Fori(0, T // 2) as i:
                for b in range(2):
                    pe.wait_ge(et_ready, 2 * i + b + 1)
                    pe.wait_ge(e_taken, free(2 * i + b))
                    for j in range(3):
                        for k in range(T):
                            last = mm(ps[:, 3 * b + j, 0:EC], ET[:, b, k, :], h[:, k, j * EC:(j + 1) * EC],
                                      start=(k == 0), stop=(k == T - 1))
                    last.then_inc(e_acc, 1)

            def gate(t):
                pe.wait_ge(xT_ready, F0 + t + 2)
                for k in range(KD):
                    last = mm(ps[:, 5, t * NE:(t + 1) * NE], xT2[:, t, k, :], wg[:, k, :],
                              start=(k == 0), stop=(k == KD - 1))
                last.then_inc(gate_acc, 1)

            pe.wait_ge(ld_small, 64)
            pe.wait_ge(e_taken, done(T - 1))
            turn(F0, 0)
            for t in range(1, T):
                turn(F0 + t, t % 2)
                gate(t - 1)
            gate(T - 1)
            with pe.Fori(0, NE // 2) as i:
                for b in range(2):
                    pe.wait_ge(ld_w1[b], 16 * (i + 1))
                    for t in range(T):
                        m = T * (2 * i + b) + t
                        pe.wait_ge(up_taken, free(m))
                        for k in range(KD):
                            mm(ps[:, t % 5, :], xT2[:, t, k, :], W1[:, b, k, :], start=(k == 0), stop=False)
                        mm(ps[:, t % 5, :], ones_row[:, :], b1_row[:, bass.ds((2 * i + b) * H2, H2)],
                           start=False, stop=True).then_inc(up_acc, 1)
            pe.wait_ge(G_ready, 1)
            pe.wait_ge(ld_wo, 16)
            for t in range(T):
                if t >= 2:
                    pe.wait_ge(gt_ready, t - 1)
                for k in range(KH):
                    last = nc.tensor.transpose(ps[:, 6 + t % 2, k * P:(k + 1) * P], G[:, t, k * P:(k + 1) * P], ident[:, :])
                last.then_inc(gt_acc, 1)
                pe.wait_ge(gt_ready, t + 1)
                if t >= 2:
                    pe.wait_ge(down_taken, t - 1)
                product(2 * (t % 2), lambda k: GT[:, t % 2, k, :], Wo, KH).then_inc(down_acc, 1)

            pe.wait_ge(down_taken, T)
            pe.wait_ge(wt_ready, 2)
            token_loop(N0, WTg, n_taken, n_acc)

            def gates_and_keys(t, b):
                pe.wait_ge(mix_ready, t + 1)
                pe.wait_ge(r_gate, t + 1)
                product(0, lambda k: xr[:, b, k, :], Wr, KD).then_inc(r_acc, 1)
                pe.wait_ge(k_act, t + 1)
                product(2, lambda k: xk[:, b, k, :], Wk, KD).then_inc(k_acc, 1)

            def turn_keys(t):
                pe.wait_ge(k_act, t + 2)
                pe.wait_ge(v_taken, t + 1)
                for k in range(KD):
                    last = nc.tensor.transpose(ps[:, 4 + k // 4, (k % 4) * P:(k % 4 + 1) * P],
                                               kact[:, k * P:(k + 1) * P], ident[:, :])
                last.then_inc(kt_acc, 1)

            def values(t):
                pe.wait_ge(kt_ready, t + 1)
                product(4, lambda k: kT[:, k, :], Wv, KD).then_inc(v_acc, 1)

            pe.wait_ge(n_taken, done(T - 1))
            for s in (ld_wr, ld_wk, ld_wv):
                pe.wait_ge(s, 16)
            turn(R0, 0)
            turn(R0 + 1, 1)
            gates_and_keys(0, 0)
            with pe.Fori(0, T // 2 - 1) as i:
                for j in range(2):
                    turn(R0 + 2 * i + j + 2, j)
                    turn_keys(2 * i + j)
                    gates_and_keys(2 * i + j + 1, (j + 1) % 2)
                    values(2 * i + j)
            turn_keys(T - 2)
            gates_and_keys(T - 1, 1)
            values(T - 2)
            turn_keys(T - 1)
            values(T - 1)


EDGES_PER_CHUNK = 125
CHUNKS_PER_STEP = 2


def kernel(x, src, dst, edge_weight, L0_gnn_W, L0_gnn_a, L0_ffn_Wg, L0_ffn_W1, L0_ffn_b1, L0_ffn_Wo, L0_ffn_bo,
           L1_gnn_bias, L1_ffn_W_r, L1_ffn_W_k, L1_ffn_W_v, L1_ffn_mu_r, L1_ffn_mu_k):
    import concourse.bacc as bacc
    from concourse.bass_utils import run_bass_kernel_spmd

    def columns(e):
        return np.ascontiguousarray(np.asarray(e).reshape(-1, EDGES_PER_CHUNK).T)

    def turned(w):
        return np.ascontiguousarray(np.swapaxes(np.asarray(w), -1, -2))

    arrays = {
        "x": np.asarray(x),
        "src_cols": columns(src),
        "dst_cols": columns(dst),
        "dst_rows": np.asarray(dst).reshape(-1, EDGES_PER_CHUNK * CHUNKS_PER_STEP),
        "ew_cols": columns(edge_weight),
        "w0": np.asarray(L0_gnn_W),
        "a": np.asarray(L0_gnn_a),
        "wg_t": turned(L0_ffn_Wg),
        "w1_t": turned(L0_ffn_W1),
        "b1": np.asarray(L0_ffn_b1),
        "wo_t": turned(L0_ffn_Wo),
        "bo": np.asarray(L0_ffn_bo).reshape(1, -1),
        "bias": np.asarray(L1_gnn_bias).reshape(1, -1),
        "wr_t": turned(L1_ffn_W_r),
        "wk_t": turned(L1_ffn_W_k),
        "wv_t": turned(L1_ffn_W_v),
        "mu_r": turned(np.asarray(L1_ffn_mu_r).reshape(-1, P)),
        "mu_k": turned(np.asarray(L1_ffn_mu_k).reshape(-1, P)),
    }
    nc = bacc.Bacc("TRN2", target_bir_lowering=False, num_devices=1)
    args = [nc.dram_tensor(n, v.shape, mybir.dt.from_np(v.dtype), kind="ExternalInput").ap() for n, v in arrays.items()]
    out = nc.dram_tensor("out", x.shape, F32, kind="ExternalOutput").ap()
    gnn_ffn_kernel(nc, *args, out)
    r = run_bass_kernel_spmd(nc, [arrays], core_ids=[0])
    return r.results[0]["out"]
```
